# Optimizing a Trainium2 kernel written in Bass

```python
import numpy as np
import jax
import jax.numpy as jnp

def _softmax(x, axis=-1):
    return jax.nn.softmax(x, axis=axis)
def _gelu(x):
    return jax.nn.gelu(x, approximate=True)
def _silu(x):
    return jax.nn.silu(x)
def _sigmoid(x):
    return jax.nn.sigmoid(x)
def _layernorm(x, axis=-1, eps=1e-5):
    m = jnp.mean(x, axis=axis, keepdims=True)
    v = jnp.var(x, axis=axis, keepdims=True)
    return (x - m) / jnp.sqrt(v + eps)
def _scatter_add(tgt, idx, src, axis=0):
    return tgt.at[idx].add(src)
def _segment_sum(src, seg, n):
    return jax.ops.segment_sum(src, seg, n)

kernel_name = 'mk_conv_preact_d1_conv_nchw128_cd1720'

def setup_inputs(seed: int = 0):
    np.random.seed(seed)
    _w = jnp.asarray
    def _rec_inputs():
        import jax
        import jax.numpy as jnp
        _gk = jax.random.key(seed)
        x = -9.26e-05 + 0.9999 * jax.random.normal(jax.random.fold_in(_gk, 1), (32, 128, 96, 96), jnp.float32)
        return x
    x = _rec_inputs()
    def _L0_conv_setup():
        import jax, jax.numpy as jnp
        import numpy as np

        def _grid_edges(h, w):
            idx = np.arange(h * w).reshape(h, w)
            down_src, down_dst = (idx[:-1, :].ravel(), idx[1:, :].ravel())
            right_src, right_dst = (idx[:, :-1].ravel(), idx[:, 1:].ravel())
            loop = np.arange(h * w)
            src = np.concatenate([down_src, right_src, loop])
            dst = np.concatenate([down_dst, right_dst, loop])
            return (jnp.asarray(src, dtype=jnp.int32), jnp.asarray(dst, dtype=jnp.int32))
        key = jax.random.key(seed)
        ks = jax.random.split(key, 5)
        b, c, h, w = (32, 128, 96, 96)
        r = 16
        x = jax.random.normal(ks[0], (b, c, h, w), dtype=jnp.float32)
        w_fc1 = jax.random.normal(ks[1], (c // r, c), dtype=jnp.float32) * 0.001
        w_fc2 = jax.random.normal(ks[2], (c, c // r), dtype=jnp.float32) * 0.001
        gcn_w = jax.random.normal(ks[3], (c, c), dtype=jnp.float32) * (1.0 / np.sqrt(c))
        gcn_b = jnp.zeros((c,), dtype=jnp.float32)
        return {'x': x, 'w_fc1': w_fc1, 'w_fc2': w_fc2, 'gcn_w': gcn_w, 'gcn_b': gcn_b}
    _L0_conv_all = _L0_conv_setup()
    _L0_conv_in = {k: v for k, v in _L0_conv_all.items() if k in ('w_fc1', 'w_fc2', 'gcn_w', 'gcn_b', )}
    del _L0_conv_all

    return {
        "x": x,
        "L0_conv_w_fc1": _L0_conv_in["w_fc1"],
        "L0_conv_w_fc2": _L0_conv_in["w_fc2"],
        "L0_conv_gcn_w": _L0_conv_in["gcn_w"],
        "L0_conv_gcn_b": _L0_conv_in["gcn_b"],
    }

def reference(x, L0_conv_w_fc1, L0_conv_w_fc2, L0_conv_gcn_w, L0_conv_gcn_b):
    import jax
    import jax.numpy as jnp
    def _L0_conv_ref(x, w_fc1, w_fc2, gcn_w, gcn_b):
        import jax, jax.numpy as jnp
        import numpy as np

        def _grid_edges(h, w):
            idx = np.arange(h * w).reshape(h, w)
            down_src, down_dst = (idx[:-1, :].ravel(), idx[1:, :].ravel())
            right_src, right_dst = (idx[:, :-1].ravel(), idx[:, 1:].ravel())
            loop = np.arange(h * w)
            src = np.concatenate([down_src, right_src, loop])
            dst = np.concatenate([down_dst, right_dst, loop])
            return (jnp.asarray(src, dtype=jnp.int32), jnp.asarray(dst, dtype=jnp.int32))
        b, c, h, w = x.shape
        n = h * w
        y = x.mean(axis=(2, 3))
        y = jax.nn.sigmoid(jax.nn.relu(y @ w_fc1.T) @ w_fc2.T)
        xg = x * y[:, :, None, None]
        src, dst = _grid_edges(h, w)
        ones = jnp.ones(src.shape, dtype=x.dtype)
        deg = jax.ops.segment_sum(ones, dst, num_segments=n)
        dinv = jnp.where(deg > 0, jax.lax.rsqrt(deg), 0.0)
        norm = dinv[src] * dinv[dst]
        xf = xg.reshape(b, c, n).transpose(0, 2, 1)
        xw = xf @ gcn_w
        msg = xw[:, src, :] * norm[None, :, None]
        agg = jax.vmap(lambda m: jax.ops.segment_sum(m, dst, num_segments=n))(msg)
        out = agg + gcn_b
        return out.transpose(0, 2, 1).reshape(b, c, h, w)

    def _gn(v, G=32, eps=1e-5):
        B_, C_, H_, W_ = v.shape
        g = v.reshape(B_, G, C_ // G, H_, W_)
        m = jnp.mean(g, axis=(2, 3, 4), keepdims=True)
        s = jnp.var(g, axis=(2, 3, 4), keepdims=True)
        return ((g - m) / jnp.sqrt(s + eps)).reshape(v.shape)

    def _ln_c(v, eps=1e-6):
        m = jnp.mean(v, axis=1, keepdims=True)
        s = jnp.var(v, axis=1, keepdims=True)
        return (v - m) / jnp.sqrt(s + eps)

    def _ln_t(v, eps=1e-5):
        m = jnp.mean(v, axis=-1, keepdims=True)
        s = jnp.var(v, axis=-1, keepdims=True)
        return (v - m) / jnp.sqrt(s + eps)

    def _to_tokens(v):
        B_, C_, H_, W_ = v.shape
        return v.reshape(B_, C_, H_ * W_).transpose(0, 2, 1)
    def _from_tokens(t, like):
        B_, C_, H_, W_ = like.shape
        return t.transpose(0, 2, 1).reshape(B_, C_, H_, W_)

    x = x + _L0_conv_ref(_gn(x), L0_conv_w_fc1, L0_conv_w_fc2, L0_conv_gcn_w, L0_conv_gcn_b)
    return x


_drawn_inputs = setup_inputs


def setup_inputs(seed=0):
    import zlib

    import numpy as np

    out = dict(_drawn_inputs(seed))
    spreads = {'L0_conv_gcn_b': (0.0, 0.1)}
    factors = {}
    for name, (base, spread) in spreads.items():
        noise = np.random.default_rng([zlib.crc32(name.encode()), seed]).standard_normal(out[name].shape)
        drawn = base * np.exp(spread * noise) if base else spread * noise
        out[name] = jnp.asarray(drawn.astype(out[name].dtype))
    for name, factor in factors.items():
        out[name] = (out[name] * factor).astype(out[name].dtype)
    return out
```

```python
import numpy as np
import concourse.bass as bass
from concourse import mybir
from contextlib import ExitStack

IMAGES, CH, H, W = 32, 128, 96, 96
GROUP = 4
PIX = H * W
EPS = 1e-5
SQUEEZE = 16
HID = CH // SQUEEZE


def gated_grid_gcn(nc, x_dram, fc1_dram, fc2_dram, gcn_w_dram, gcn_b_dram, mean_mix_dram, dev_mix_dram, eye_dram, out_dram):
    fp32 = mybir.dt.float32
    bf16 = mybir.dt.bfloat16
    ALU = mybir.AluOpType
    ACT = mybir.ActivationFunctionType

    SLOTS = 4
    CHUNKS = 6
    ROWS = H // CHUNKS
    CPIX = ROWS * W
    BANK = 512
    BANKS = CPIX // BANK
    THIRDS = 3
    TPIX = PIX // THIRDS
    TROWS = H // THIRDS
    PE_ADDS_X = (2, 5)
    SBUFS = 3
    K_EDGE = float(np.sqrt(1.5) - 1.0)
    K_CORNER = float(np.sqrt(4.5) - 1.5)

    def on_act(k):
        return k in PE_ADDS_X

    def evacs(k, act):
        return sum(on_act(c) == act for c in range(k + 1))

    ACT_EVACS, DVE_EVACS = evacs(CHUNKS - 1, True), evacs(CHUNKS - 1, False)

    ctx = ExitStack()
    with ctx:
        def sb(name, shape, dt=fp32):
            return ctx.enter_context(nc.sbuf_tensor(name, shape, dt))

        def sem(name):
            return ctx.enter_context(nc.semaphore(name))

        x_ring = sb("x_ring", [CH, SLOTS * PIX])
        s_buf = [sb(f"s_buf{n}", [CH, CPIX]) for n in range(SBUFS)]
        junk_x = [sb(f"junk_x{n}", [CH, TPIX], bf16) for n in range(2)]
        junk_xx = [sb(f"junk_xx{n}", [CH, TPIX], bf16) for n in range(2)]
        gcn_w = sb("gcn_w", [CH, CH])
        w_scaled = [sb(f"w_scaled{n}", [CH, CH]) for n in range(2)]
        w_plus_eye = [sb(f"w_plus_eye{n}", [CH, CH]) for n in range(2)]
        eye = sb("eye", [CH, CH])
        mean_mix = sb("mean_mix", [CH, CH])
        dev_mix = sb("dev_mix", [CH, CH])
        fc1 = sb("fc1", [CH, HID])
        fc2 = sb("fc2", [HID, CH])
        gcn_b = sb("gcn_b", [CH, 1])
        sums = sb("sums", [CH, SLOTS * THIRDS])
        squares = sb("squares", [CH, SLOTS * THIRDS])
        moments = sb("moments", [CH, SLOTS * 2])
        var = sb("var", [CH, 1])
        logv = sb("logv", [CH, 1])
        guess = sb("guess", [CH, 1])
        vgg = sb("vgg", [CH, 1])
        newton = sb("newton", [CH, 1])
        rstd = sb("rstd", [CH, 1])
        pooled = sb("pooled", [CH, 1])
        hidden = sb("hidden", [HID, 1])
        expz = sb("expz", [CH, 1])
        expz1 = sb("expz1", [CH, 1])
        gate = sb("gate", [CH, 1])
        scale = sb("scale", [CH, 1])
        bias = [sb(f"bias{n}", [CH, 1]) for n in range(2)]
        edge = [sb(f"edge{n}", [CH, H, 2]) for n in range(2)]
        top = [sb(f"top{n}", [CH, 2, W]) for n in range(2)]

        half_col = sb("half_col", [CH, H])
        row_15 = sb("row_15", [CH, W])
        corner = sb("corner", [CH, 1])

        ps = ctx.enter_context(nc.psum_tensor("ps", [CH, 2 * BANKS * BANK], fp32))
        ps_mean = ctx.enter_context(nc.psum_tensor("ps_mean", [CH, BANK], fp32))
        ps_gate = ctx.enter_context(nc.psum_tensor("ps_gate", [CH, BANK], fp32))

        params_in = sem("params_in")
        x_in = [sem(f"x_in{j}") for j in range(THIRDS)]
        out_stored = [sem(f"out_stored{j}") for j in range(THIRDS)]
        sums_done = sem("sums_done")
        mean_mixed = sem("mean_mixed")
        moments_ready = sem("moments_ready")
        squares_done = sem("squares_done")
        var_mixed = sem("var_mixed")
        var_ready = sem("var_ready")
        log_ready = sem("log_ready")
        guess_ready = sem("guess_ready")
        rstd_steps = sem("rstd_steps")
        pooled_ready = sem("pooled_ready")
        hidden_mixed = sem("hidden_mixed")
        hidden_ready = sem("hidden_ready")
        gate_mixed = sem("gate_mixed")
        expz_ready = sem("expz_ready")
        gate_steps = sem("gate_steps")
        w_ready = sem("w_ready")
        bias_mixed = sem("bias_mixed")
        bias_ready = sem("bias_ready")
        edge_steps = sem("edge_steps")
        vertical_done = sem("vertical_done")
        s_summed = sem("s_summed")
        s_ready = sem("s_ready")
        chunk_mixed = sem("chunk_mixed")
        out_ready = [sem(f"out_ready{k}") for k in range(CHUNKS)]

        N_PARAMS = 7 * 16

        def x_flat(u, pixel, n):
            return x_ring[:, u % SLOTS * PIX + pixel:u % SLOTS * PIX + pixel + n]

        def x_rows(u, row, n):
            return x_flat(u, row * W, n * W).rearrange("p (r w) -> p r w", w=W)

        def s_rows(k):
            return s_buf[k % SBUFS][:, :].rearrange("p (r w) -> p r w", w=W)

        def ps_half(k):
            return ps[:, (k % 2) * CPIX:(k % 2 + 1) * CPIX]

        def column(buf, u, width, n=0):
            return buf[:, u % SLOTS * width + n:u % SLOTS * width + n + 1]

        def for_images(eng, image):
            for u in range(SLOTS):
                image(u, u, u == 0, False, False)
            with eng.Fori(1, IMAGES // SLOTS - 1) as group:
                for u in range(SLOTS):
                    image(group * SLOTS + u, u, False, False, False)
            for u in range(SLOTS):
                image(IMAGES - SLOTS + u, u, False, u >= SLOTS - 2, u == SLOTS - 1)

        block = ctx.enter_context(nc.Block())

        @block.sync
        def _(sp):
            def third(dram, t, j):
                return dram[bass.ds(t, 1), :, j * TPIX:(j + 1) * TPIX].rearrange("a c n -> c (a n)")

            def load(t, u, j):
                sp.dma_start(x_flat(u, j * TPIX, TPIX), third(x_dram, t, j)).then_inc(x_in[j], 16)

            def store(t, u, j):
                sp.dma_start(third(out_dram, t, j), x_flat(u, j * TPIX, TPIX)).then_inc(out_stored[j], 16)

            for j in range(THIRDS):
                load(0, 0, j)
            for dst, src in ((gcn_w, gcn_w_dram), (eye, eye_dram), (mean_mix, mean_mix_dram), (dev_mix, dev_mix_dram),
                             (fc1, fc1_dram), (fc2, fc2_dram), (gcn_b, gcn_b_dram)):
                sp.dma_start(dst[:, :], src).then_inc(params_in, 16)
            for t in range(1, SLOTS):
                for j in range(THIRDS):
                    sp.wait_ge(x_in[j], 16 * t)
                    load(t, t, j)

            def image(t, u, first, no_second, no_next):
                loads = not isinstance(t, int) or not first and t + SLOTS - 1 < IMAGES
                for j in range(THIRDS):
                    if loads:
                        sp.wait_ge(x_in[j], t * 16 + (SLOTS - 1) * 16)
                    if not first:
                        sp.wait_ge(out_stored[j], t * 16)
                    if loads:
                        load(t + SLOTS - 1, u - 1, j)
                    for k in range(CHUNKS):
                        if k * THIRDS // CHUNKS == j:
                            sp.wait_ge(out_ready[k], t + 1)
                    store(t, u, j)

            for_images(sp, image)
            for j in range(THIRDS):
                sp.wait_ge(out_stored[j], 16 * IMAGES)

        @block.scalar
        def _(act):
            nc.scalar.preload_act_table_set("natural_log_exp_and_others")

            def sum_third(t, u, j):
                act.wait_ge(x_in[j], t * 16 + 16)
                if not isinstance(t, int) or t * THIRDS + j >= 2:
                    act.wait_ge(sums_done, t * THIRDS + j - 1)
                nc.scalar.activation(junk_x[(u + j) % 2][:, :], x_flat(u, j * TPIX, TPIX), ACT.Identity,
                                     accum_out=column(sums, u, THIRDS, j)).then_inc(sums_done, 1)

            def take_moments(t, u):
                act.wait_ge(mean_mixed, t + 1)
                nc.scalar.copy(moments[:, u % SLOTS * 2:u % SLOTS * 2 + 2], ps_mean[:, 0:2]).then_inc(moments_ready, 1)

            def square_third(t, u, j):
                if j == 0:
                    act.wait_ge(moments_ready, t + 1)
                if not isinstance(t, int) or t * THIRDS + j >= 2:
                    act.wait_ge(squares_done, t * THIRDS + j - 1)
                nc.scalar.activation(junk_xx[(u + j) % 2][:, :], x_flat(u, j * TPIX, TPIX), ACT.Square,
                                     bias=column(moments, u, 2),
                                     accum_out=column(squares, u, THIRDS, j)).then_inc(squares_done, 1)

            def guess_rstd(t):
                act.wait_ge(var_ready, t + 1)
                nc.scalar.activation(logv[:, :], var[:, :], ACT.Ln).then_inc(log_ready, 1)
                act.wait_ge(log_ready, t + 1)
                nc.scalar.activation(guess[:, :], logv[:, :], ACT.Exp, scale=-0.5).then_inc(guess_ready, 1)

            def exp_gate(t):
                act.wait_ge(gate_mixed, t + 1)
                nc.scalar.activation(expz[:, :], ps_gate[:, 2:3], ACT.Exp, scale=-1.0).then_inc(expz_ready, 1)

            def evacuate(t, u, k):
                g = t * CHUNKS + k
                act.wait_ge(chunk_mixed, g + 1)
                act.wait_ge(bias_ready, t + 1)
                if k < CHUNKS - 1:
                    act.wait_ge(s_summed, g + 2)
                nc.scalar.activation(x_flat(u, k * CPIX, CPIX), ps_half(k), ACT.Identity,
                                     bias=bias[u % 2][:, :]).then_inc(out_ready[k], 1)

            for t in (0, 1):
                for j in range(THIRDS):
                    sum_third(t, t, j)
                take_moments(t, t)
                if t == 0:
                    for j in range(THIRDS):
                        square_third(0, 0, j)
                    guess_rstd(0)
                    exp_gate(0)

            def image(t, u, first, no_second, no_next):
                if not first:
                    evacuate(t - 1, u - 1, 5)
                if not no_next:
                    square_third(t + 1, u + 1, 0)
                    square_third(t + 1, u + 1, 1)
                    square_third(t + 1, u + 1, 2)
                if not no_second:
                    sum_third(t + 2, u + 2, 0)
                if not no_next:
                    guess_rstd(t + 1)
                evacuate(t, u, 2)
                if not no_second:
                    sum_third(t + 2, u + 2, 1)
                if not no_next:
                    exp_gate(t + 1)
                if not no_second:
                    sum_third(t + 2, u + 2, 2)
                    take_moments(t + 2, u + 2)

            for_images(act, image)
            evacuate(IMAGES - 1, SLOTS - 1, 5)

        @block.gpsimd
        def _(pool):
            EDGE_STEPS = 10

            def edges(t, u):
                e, r = edge[u % 2], top[u % 2]
                mean = column(moments, u, 2)
                pool.wait_ge(moments_ready, t + 1)
                for j in range(THIRDS):
                    pool.wait_ge(x_in[j], t * 16 + 16)
                col = x_rows(u, 0, H)[:, :, 0]
                row = x_rows(u, 0, 1)[:, 0, :]
                nc.gpsimd.tensor_tensor(corner[:, :], row[:, 0:1], mean, ALU.add).then_inc(edge_steps, 1)
                nc.gpsimd.tensor_scalar(half_col[:, :], col, 0.5, 0.0, ALU.mult, ALU.add).then_inc(edge_steps, 1)
                nc.gpsimd.tensor_scalar(e[:, 1:H, 1], col[:, 1:H], mean, K_EDGE, ALU.add, ALU.mult).then_inc(edge_steps, 1)
                nc.gpsimd.tensor_scalar(row_15[:, :], row, 1.5, 0.0, ALU.mult, ALU.add).then_inc(edge_steps, 1)
                nc.gpsimd.tensor_scalar(r[:, 0, 0:1], row[:, 0:1], 3.0, 0.0, ALU.mult, ALU.add).then_inc(edge_steps, 1)
                nc.gpsimd.tensor_scalar(r[:, 1, 1:W], row[:, 1:W], mean, K_EDGE, ALU.add, ALU.mult).then_inc(edge_steps, 1)
                pool.wait_ge(edge_steps, t * EDGE_STEPS + 6)
                nc.gpsimd.tensor_tensor(e[:, 1:H, 0], half_col[:, 1:H], half_col[:, 0:H - 1], ALU.add).then_inc(edge_steps, 1)
                nc.gpsimd.tensor_tensor(r[:, 0, 1:W], row_15[:, 1:W], row_15[:, 0:W - 1], ALU.add).then_inc(edge_steps, 1)
                nc.gpsimd.tensor_scalar(r[:, 1, 0:1], corner[:, :], K_CORNER, 0.0, ALU.mult, ALU.add).then_inc(edge_steps, 1)
                pool.wait_ge(edge_steps, t * EDGE_STEPS + 9)
                nc.gpsimd.tensor_tensor(r[:, 0, 1:2], r[:, 0, 1:2], r[:, 1, 0:1], ALU.add).then_inc(edge_steps, 1)

            def edges_up(t, u):
                pool.wait_ge(edge_steps, t * EDGE_STEPS + EDGE_STEPS)
                for k in PE_ADDS_X:
                    cells = edge[u % 2][:, k * ROWS:(k + 1) * ROWS, 0]
                    nc.gpsimd.tensor_tensor(cells, cells, x_rows(u, k * ROWS - 1, ROWS)[:, :, 0],
                                            ALU.add).then_inc(edges_done, 1)
                pool.wait_ge(edges_done, t * len(PE_ADDS_X) + len(PE_ADDS_X))

            edges_done = sem("edges_done")
            top_fixed = sem("top_fixed")

            def fix(t, u, k):
                g = t * CHUNKS + k
                s = s_rows(k)
                e = edge[u % 2][:, k * ROWS:(k + 1) * ROWS, :]
                pool.wait_ge(s_summed, g + 1)
                if k == 0:
                    nc.gpsimd.tensor_tensor(s[:, 1:ROWS, 0:2], s[:, 1:ROWS, 0:2], e[:, 1:ROWS, :], ALU.add).then_inc(top_fixed, 1)
                    nc.gpsimd.tensor_copy(s[:, 0, :], top[u % 2][:, 0, :]).then_inc(top_fixed, 1)
                    pool.wait_ge(top_fixed, t * 2 + 2)
                    nc.gpsimd.tensor_tensor(s[:, 1, :], s[:, 1, :], top[u % 2][:, 1, :], ALU.add).then_inc(s_ready, 1)
                elif on_act(k):
                    nc.gpsimd.tensor_tensor(s[:, :, 1], s[:, :, 1], e[:, :, 1], ALU.add).then_inc(s_ready, 1)
                    nc.gpsimd.tensor_copy(s[:, :, 0], e[:, :, 0]).then_inc(s_ready, 1)
                else:
                    nc.gpsimd.tensor_tensor(s[:, :, 0:2], s[:, :, 0:2], e, ALU.add).then_inc(s_ready, 1)

            edges(0, 0)
            edges_up(0, 0)

            def image(t, u, first, no_second, no_next):
                for k in range(CHUNKS):
                    fix(t, u, k)
                    if k == 0 and not no_next:
                        edges(t + 1, u + 1)
                    if k == 1 and not no_next:
                        edges_up(t + 1, u + 1)

            for_images(pool, image)

        @block.vector
        def _(dve):
            def vertical(t, u, k):
                g = t * CHUNKS + k
                s = s_rows(k)
                dve.wait_ge(x_in[k * THIRDS // CHUNKS], t * 16 + 16)
                if not isinstance(t, int) or g >= SBUFS:
                    dve.wait_ge(chunk_mixed, g - SBUFS + 1)
                if on_act(k):
                    nc.vector.tensor_tensor(s[:, :, 1:W], x_rows(u, k * ROWS - 1, ROWS)[:, :, 1:W],
                                            x_rows(u, k * ROWS, ROWS)[:, :, 0:W - 1], ALU.add).then_inc(s_summed, 1)
                else:
                    skip = W if k == 0 else 0
                    nc.vector.tensor_tensor(s_buf[k % SBUFS][:, skip:CPIX], x_flat(u, k * CPIX + skip, CPIX - skip),
                                            x_flat(u, k * CPIX + skip - W, CPIX - skip), ALU.add).then_inc(vertical_done, 1)

            def horizontal(t, u, k):
                if on_act(k):
                    return
                s = s_rows(k)
                skip = 1 if k == 0 else 0
                dve.wait_ge(vertical_done, t * DVE_EVACS + evacs(k, False))
                cells = s[:, skip:ROWS, 1:W]
                nc.vector.tensor_tensor(cells, cells, x_rows(u, k * ROWS + skip, ROWS - skip)[:, :, 0:W - 1],
                                        ALU.add).then_inc(s_summed, 1)

            def evacuate(t, u, k):
                if on_act(k):
                    return
                dve.wait_ge(chunk_mixed, t * CHUNKS + k + 1)
                if k == 0:
                    dve.wait_ge(bias_ready, t + 1)
                if k < CHUNKS - 1:
                    dve.wait_ge(s_summed, t * CHUNKS + k + 2)
                cells = x_flat(u, k * CPIX, CPIX)
                nc.vector.scalar_tensor_tensor(out=cells, in0=ps_half(k), scalar=bias[u % 2][:, :], in1=cells,
                                               op0=ALU.add, op1=ALU.add).then_inc(out_ready[k], 1)

            def take_var(t):
                dve.wait_ge(var_mixed, t + 1)
                nc.vector.tensor_scalar(var[:, :], ps_gate[:, 0:1], -1.0, EPS, ALU.mult, ALU.add).then_inc(var_ready, 1)

            def refine_rstd(t, u):
                dve.wait_ge(guess_ready, t + 1)
                nc.vector.scalar_tensor_tensor(out=vgg[:, :], in0=guess[:, :], scalar=guess[:, :], in1=var[:, :],
                                               op0=ALU.mult, op1=ALU.mult).then_inc(rstd_steps, 1)
                dve.wait_ge(rstd_steps, t * 3 + 1)
                nc.vector.tensor_scalar(newton[:, :], vgg[:, :], -0.5, 1.5, ALU.mult, ALU.add).then_inc(rstd_steps, 1)
                dve.wait_ge(rstd_steps, t * 3 + 2)
                nc.vector.tensor_tensor(rstd[:, :], guess[:, :], newton[:, :], ALU.mult).then_inc(rstd_steps, 1)
                dve.wait_ge(rstd_steps, t * 3 + 3)
                nc.vector.tensor_tensor(pooled[:, :], rstd[:, :], column(moments, u, 2, 1), ALU.mult).then_inc(pooled_ready, 1)

            def take_hidden(t):
                dve.wait_ge(hidden_mixed, t + 1)
                nc.vector.tensor_scalar(hidden[:, :], ps_gate[0:HID, 1:2], 0.0, None, ALU.max).then_inc(hidden_ready, 1)

            def scale_weights(t, u):
                dve.wait_ge(expz_ready, t + 1)
                nc.vector.tensor_scalar(expz1[:, :], expz[:, :], 1.0, None, ALU.add).then_inc(gate_steps, 1)
                dve.wait_ge(gate_steps, t * 3 + 1)
                nc.vector.reciprocal(gate[:, :], expz1[:, :]).then_inc(gate_steps, 1)
                dve.wait_ge(gate_steps, t * 3 + 2)
                nc.vector.tensor_scalar(scale[:, :], gate[:, :], rstd[:, :], 1.0 / 3.0, ALU.mult, ALU.mult).then_inc(gate_steps, 1)
                dve.wait_ge(gate_steps, t * 3 + 3)
                if not isinstance(t, int) or t >= 2:
                    dve.wait_ge(chunk_mixed, (t - 1) * CHUNKS)
                nc.vector.tensor_scalar(w_scaled[u % 2][:, :], gcn_w[:, :], scale[:, :], None, ALU.mult).then_inc(w_ready, 1)
                nc.vector.scalar_tensor_tensor(out=w_plus_eye[u % 2][:, :], in0=gcn_w[:, :], scalar=scale[:, :],
                                               in1=eye[:, :], op0=ALU.mult, op1=ALU.add).then_inc(w_ready, 1)

            def take_bias(t, u):
                dve.wait_ge(bias_mixed, t + 1)
                nc.vector.tensor_scalar(bias[u % 2][:, :], ps_gate[:, 3:4], 3.0, gcn_b[:, :], ALU.mult,
                                        ALU.add).then_inc(bias_ready, 1)

            dve.wait_ge(params_in, N_PARAMS)
            take_var(0)
            refine_rstd(0, 0)
            take_hidden(0)
            scale_weights(0, 0)
            take_bias(0, 0)

            def image(t, u, first, no_second, no_next):
                for k in range(CHUNKS):
                    vertical(t, u, k)
                    if k >= 2:
                        evacuate(t, u, k - 2)
                    elif not first:
                        evacuate(t - 1, u - 1, k + CHUNKS - 2)
                    horizontal(t, u, k)
                    if not no_next:
                        if k == 3:
                            take_var(t + 1)
                        if k == 4:
                            refine_rstd(t + 1, u + 1)
                        if k == 5:
                            take_hidden(t + 1)
                            scale_weights(t + 1, u + 1)
                            take_bias(t + 1, u + 1)

            for_images(dve, image)
            evacuate(IMAGES - 1, SLOTS - 1, 4)

        @block.tensor
        def _(pe):
            def mix_mean(t, u):
                pe.wait_ge(sums_done, t * THIRDS + THIRDS)
                if not isinstance(t, int) or t:
                    pe.wait_ge(moments_ready, t)
                for n, mix in enumerate((mean_mix, dev_mix)):
                    for j in range(THIRDS):
                        last = nc.tensor.matmul(ps_mean[:, n:n + 1], mix[:, :], column(sums, u, THIRDS, j),
                                                start=j == 0, stop=j == THIRDS - 1)
                last.then_inc(mean_mixed, 1)

            def mix_var(t, u):
                pe.wait_ge(squares_done, t * THIRDS + THIRDS)
                if not isinstance(t, int) or t:
                    pe.wait_ge(bias_ready, t)
                for j in range(THIRDS):
                    last = nc.tensor.matmul(ps_gate[:, 0:1], mean_mix[:, :], column(squares, u, THIRDS, j),
                                            start=j == 0, stop=j == THIRDS - 1)
                last.then_inc(var_mixed, 1)

            def mix_hidden(t):
                pe.wait_ge(pooled_ready, t + 1)
                nc.tensor.matmul(ps_gate[0:HID, 1:2], fc1[:, :], pooled[:, :], start=True, stop=True).then_inc(hidden_mixed, 1)

            def mix_gate(t):
                pe.wait_ge(hidden_ready, t + 1)
                nc.tensor.matmul(ps_gate[:, 2:3], fc2[:, :], hidden[:, :], start=True, stop=True).then_inc(gate_mixed, 1)

            def mix_bias(t, u):
                pe.wait_ge(w_ready, t * 2 + 2)
                nc.tensor.matmul(ps_gate[:, 3:4], w_scaled[u % 2][:, :], column(moments, u, 2), start=True,
                                 stop=True).then_inc(bias_mixed, 1)

            def mix_chunk(t, u, k, first, after):
                g = t * CHUNKS + k
                pe.wait_ge(s_ready, t * (CHUNKS + ACT_EVACS) + k + 1 + evacs(k, True))
                if k >= 2:
                    before, image = k - 2, t
                else:
                    before, image = k + CHUNKS - 2, t - 1
                if k >= 2 or not first:
                    pe.wait_ge(out_ready[before], image + 1)
                half = ps_half(k)
                for b in range(BANKS):
                    bank = half[:, b * BANK:(b + 1) * BANK]
                    last = nc.tensor.matmul(bank, w_scaled[u % 2][:, :], s_buf[k % SBUFS][:, b * BANK:(b + 1) * BANK],
                                            start=True, stop=not on_act(k))
                    if on_act(k):
                        last = nc.tensor.matmul(bank, w_plus_eye[u % 2][:, :], x_flat(u, k * CPIX + b * BANK, BANK),
                                                start=False, stop=True)
                    if b == BANKS - 1:
                        last.then_inc(chunk_mixed, 1)
                    for f in after.get((k, b), ()):
                        f()

            pe.wait_ge(params_in, N_PARAMS)
            mix_mean(0, 0)
            mix_var(0, 0)
            mix_hidden(0)
            mix_gate(0)
            mix_bias(0, 0)
            mix_mean(1, 1)

            def image(t, u, first, no_second, no_next):
                after = {}
                if not no_next:
                    after[(2, 0)] = [lambda: mix_var(t + 1, u + 1)]
                    after[(3, 0)] = [lambda: mix_hidden(t + 1)]
                    after[(3, 2)] = [lambda: mix_gate(t + 1)]
                    after[(4, 2)] = [lambda: mix_bias(t + 1, u + 1)]
                if not no_second:
                    after[(5, 2)] = [lambda: mix_mean(t + 2, u + 2)]
                for k in range(CHUNKS):
                    mix_chunk(t, u, k, first, after)

            for_images(pe, image)


def kernel(x, L0_conv_w_fc1, L0_conv_w_fc2, L0_conv_gcn_w, L0_conv_gcn_b):
    import concourse.bacc as bacc
    from concourse.bass_utils import run_bass_kernel_spmd

    group = np.kron(np.eye(CH // GROUP), np.ones((GROUP, GROUP))) / GROUP
    arrays = {
        "x": np.ascontiguousarray(x).reshape(IMAGES, CH, PIX),
        "fc1": np.ascontiguousarray(np.asarray(L0_conv_w_fc1).T),
        "fc2": np.ascontiguousarray(np.asarray(L0_conv_w_fc2).T),
        "gcn_w": np.ascontiguousarray(L0_conv_gcn_w),
        "gcn_b": np.ascontiguousarray(L0_conv_gcn_b).reshape(CH, 1),
        "mean_mix": (-group / PIX).astype(np.float32),
        "dev_mix": ((np.eye(CH) - group) / PIX).astype(np.float32),
        "eye": np.eye(CH, dtype=np.float32),
    }
    nc = bacc.Bacc("TRN2", target_bir_lowering=False, num_devices=1)
    args = [nc.dram_tensor("in_" + n, a.shape, mybir.dt.from_np(a.dtype), kind="ExternalInput").ap() for n, a in arrays.items()]
    out = nc.dram_tensor("out", (IMAGES, CH, PIX), mybir.dt.float32, kind="ExternalOutput").ap()
    gated_grid_gcn(nc, *args, out)
    r = run_bass_kernel_spmd(nc, [{"in_" + n: a for n, a in arrays.items()}], core_ids=[0])
    return r.results[0]["out"].reshape(IMAGES, CH, H, W)
```

```python
import numpy as np
import concourse.bass as bass
from concourse import mybir
from contextlib import ExitStack

IMAGES, CH, H, W = 32, 128, 96, 96
GROUP = 4
PIX = H * W
EPS = 1e-5
SQUEEZE = 16
HID = CH // SQUEEZE


def gated_grid_gcn(nc, x_dram, fc1_dram, fc2_dram, gcn_w_dram, gcn_b_dram, mean_mix_dram, dev_mix_dram, eye_dram, out_dram):
    fp32 = mybir.dt.float32
    bf16 = mybir.dt.bfloat16
    ALU = mybir.AluOpType
    ACT = mybir.ActivationFunctionType

    SLOTS = 4
    CHUNKS = 6
    ROWS = H // CHUNKS
    CPIX = ROWS * W
    BANK = 512
    BANKS = CPIX // BANK
    THIRDS = 3
    TPIX = PIX // THIRDS
    TROWS = H // THIRDS
    PE_ADDS_X = (1, 3, 5)
    SBUFS = 6
    LEAD = 4
    K_EDGE = float(np.sqrt(1.5) - 1.0)
    K_CORNER = float(np.sqrt(4.5) - 1.5)

    LAST_PE_ADDS_X = {IMAGES - 1: (1,)}

    def on_act(t, k):
        return k in (LAST_PE_ADDS_X.get(t, PE_ADDS_X) if isinstance(t, int) else PE_ADDS_X)

    def taken_out(t, k, act):
        before = t * sum(on_act(None, c) == act for c in range(CHUNKS))
        if isinstance(t, int):
            before = sum(on_act(i, c) == act for i in range(t) for c in range(CHUNKS))
        return before + sum(on_act(t, c) == act for c in range(k + 1))

    ctx = ExitStack()
    with ctx:
        def sb(name, shape, dt=fp32):
            return ctx.enter_context(nc.sbuf_tensor(name, shape, dt))

        def sem(name):
            return ctx.enter_context(nc.semaphore(name))

        x_ring = sb("x_ring", [CH, SLOTS * PIX])
        s_buf = [sb(f"s_buf{n}", [CH, CPIX]) for n in range(SBUFS)]
        junk_x = sb("junk_x", [CH, TPIX], bf16)
        junk_xx = sb("junk_xx", [CH, TPIX], bf16)
        gcn_w = sb("gcn_w", [CH, CH])
        w_scaled = [sb(f"w_scaled{n}", [CH, CH]) for n in range(2)]
        w_plus_eye = [sb(f"w_plus_eye{n}", [CH, CH]) for n in range(2)]
        eye = sb("eye", [CH, CH])
        mean_mix = sb("mean_mix", [CH, CH])
        dev_mix = sb("dev_mix", [CH, CH])
        fc1 = sb("fc1", [CH, HID])
        fc2 = sb("fc2", [HID, CH])
        gcn_b = sb("gcn_b", [CH, 1])
        sums = sb("sums", [CH, SLOTS * THIRDS])
        squares = sb("squares", [CH, SLOTS * THIRDS])
        moments = sb("moments", [CH, SLOTS * 2])
        thirds_mean = sb("thirds_mean", [CH, THIRDS])
        thirds_dev = sb("thirds_dev", [CH, THIRDS])
        thirds_var = sb("thirds_var", [CH, THIRDS])
        var = sb("var", [CH, 1])
        logv = sb("logv", [CH, 1])
        guess = sb("guess", [CH, 1])
        vgg = sb("vgg", [CH, 1])
        newton = sb("newton", [CH, 1])
        rstd = sb("rstd", [CH, 1])
        pooled = sb("pooled", [CH, 1])
        hidden = sb("hidden", [HID, 1])
        expz = sb("expz", [CH, 1])
        expz1 = sb("expz1", [CH, 1])
        gate = sb("gate", [CH, 1])
        scale = sb("scale", [CH, 1])
        bias = [sb(f"bias{n}", [CH, 1]) for n in range(2)]
        edge = [sb(f"edge{n}", [CH, H, 2]) for n in range(2)]
        top = [sb(f"top{n}", [CH, 2, W]) for n in range(2)]

        half_col = sb("half_col", [CH, H])
        row_15 = sb("row_15", [CH, W])
        corner = sb("corner", [CH, 1])

        ps = ctx.enter_context(nc.psum_tensor("ps", [CH, 2 * BANKS * BANK], fp32))
        ps_mean = ctx.enter_context(nc.psum_tensor("ps_mean", [CH, BANK], fp32))
        ps_gate = ctx.enter_context(nc.psum_tensor("ps_gate", [CH, BANK], fp32))

        params_in = sem("params_in")
        x_in = [sem(f"x_in{j}") for j in range(THIRDS)]
        out_stored = [sem(f"out_stored{j}") for j in range(THIRDS)]
        sums_done = sem("sums_done")
        mean_mixed = sem("mean_mixed")
        moments_ready = sem("moments_ready")
        squares_done = sem("squares_done")
        var_mixed = sem("var_mixed")
        var_ready = sem("var_ready")
        log_ready = sem("log_ready")
        guess_ready = sem("guess_ready")
        rstd_steps = sem("rstd_steps")
        pooled_ready = sem("pooled_ready")
        hidden_mixed = sem("hidden_mixed")
        hidden_ready = sem("hidden_ready")
        gate_mixed = sem("gate_mixed")
        expz_ready = sem("expz_ready")
        gate_steps = sem("gate_steps")
        w_ready = sem("w_ready")
        bias_mixed = sem("bias_mixed")
        bias_ready = sem("bias_ready")
        edge_steps = sem("edge_steps")
        edges_done = sem("edges_done")
        top_fixed = sem("top_fixed")
        vertical_done = sem("vertical_done")
        s_summed = sem("s_summed")
        s_ready = sem("s_ready")
        chunk_mixed = sem("chunk_mixed")
        out_ready = [sem(f"out_ready{k}") for k in range(CHUNKS)]

        N_PARAMS = 7 * 16

        def x_flat(u, pixel, n):
            return x_ring[:, u % SLOTS * PIX + pixel:u % SLOTS * PIX + pixel + n]

        def x_rows(u, row, n):
            return x_flat(u, row * W, n * W).rearrange("p (r w) -> p r w", w=W)

        def s_rows(k):
            return s_buf[k % SBUFS][:, :].rearrange("p (r w) -> p r w", w=W)

        def ps_half(k):
            return ps[:, (k % 2) * CPIX:(k % 2 + 1) * CPIX]

        def column(buf, u, width, n=0):
            return buf[:, u % SLOTS * width + n:u % SLOTS * width + n + 1]

        def columns(buf, u):
            return buf[:, u % SLOTS * THIRDS:(u % SLOTS + 1) * THIRDS]

        def third(dram, t, j):
            return dram[bass.ds(t, 1), :, j * TPIX:(j + 1) * TPIX].rearrange("a c n -> c (a n)")

        def for_images(eng, image):
            for u in range(SLOTS):
                image(u, u, u == 0, False, False, False)
            with eng.Fori(1, IMAGES // SLOTS - 1) as group:
                for u in range(SLOTS):
                    image(group * SLOTS + u, u, False, False, False, False)
            for u in range(SLOTS):
                image(IMAGES - SLOTS + u, u, False, u >= SLOTS - 3, u >= SLOTS - 2, u == SLOTS - 1)

        block = ctx.enter_context(nc.Block())

        @block.sync
        def _(sp):
            def load(t, u, j):
                sp.dma_start(x_flat(u, j * TPIX, TPIX), third(x_dram, t, j)).then_inc(x_in[j], 16)

            for j in range(THIRDS):
                load(0, 0, j)
            for dst, src in ((gcn_w, gcn_w_dram), (eye, eye_dram), (mean_mix, mean_mix_dram), (dev_mix, dev_mix_dram),
                             (fc1, fc1_dram), (fc2, fc2_dram), (gcn_b, gcn_b_dram)):
                sp.dma_start(dst[:, :], src).then_inc(params_in, 16)
            for t in range(1, SLOTS):
                for j in range(THIRDS):
                    sp.wait_ge(x_in[j], 16 * t)
                    load(t, t, j)

            def image(t, u, first, no_third, no_second, no_next):
                if first or isinstance(t, int) and t + SLOTS - 1 >= IMAGES:
                    return
                for j in range(THIRDS):
                    sp.wait_ge(x_in[j], t * 16 + (SLOTS - 1) * 16)
                    sp.wait_ge(out_stored[j], t * 16)
                    load(t + SLOTS - 1, u - 1, j)

            for_images(sp, image)

        @block.scalar
        def _(act):
            nc.scalar.preload_act_table_set("natural_log_exp_and_others")

            def sum_third(t, u, j):
                act.wait_ge(x_in[j], t * 16 + 16)
                act.wait_ge(sums_done, t * THIRDS + j)
                nc.scalar.activation(junk_x[:, :], x_flat(u, j * TPIX, TPIX), ACT.Identity,
                                     accum_out=column(sums, u, THIRDS, j)).then_inc(sums_done, 1)

            def take_moments(t, u):
                act.wait_ge(mean_mixed, t + 1)
                nc.scalar.activation(thirds_mean[:, :], ps_mean[:, 0:THIRDS], ACT.Identity,
                                     accum_out=column(moments, u, 2)).then_inc(moments_ready, 1)
                nc.scalar.activation(thirds_dev[:, :], ps_mean[:, THIRDS:2 * THIRDS], ACT.Identity,
                                     accum_out=column(moments, u, 2, 1)).then_inc(moments_ready, 1)

            def square_third(t, u, j):
                if j == 0:
                    act.wait_ge(moments_ready, t * 2 + 2)
                if not isinstance(t, int) or t or j:
                    act.wait_ge(squares_done, t * THIRDS + j)
                nc.scalar.activation(junk_xx[:, :], x_flat(u, j * TPIX, TPIX), ACT.Square,
                                     bias=column(moments, u, 2),
                                     accum_out=column(squares, u, THIRDS, j)).then_inc(squares_done, 1)

            def guess_rstd(t):
                act.wait_ge(var_ready, t + 1)
                nc.scalar.activation(logv[:, :], var[:, :], ACT.Ln).then_inc(log_ready, 1)
                act.wait_ge(log_ready, t + 1)
                nc.scalar.activation(guess[:, :], logv[:, :], ACT.Exp, scale=-0.5).then_inc(guess_ready, 1)

            def exp_gate(t):
                act.wait_ge(gate_mixed, t + 1)
                nc.scalar.activation(expz[:, :], ps_gate[:, 2:3], ACT.Exp, scale=-1.0).then_inc(expz_ready, 1)

            def store(t, u, j):
                if not isinstance(t, int) or t:
                    act.wait_ge(out_stored[j], t * 16)
                for k in range(CHUNKS):
                    if k * THIRDS // CHUNKS == j:
                        act.wait_ge(out_ready[k], t + 1)
                act.dma_start(third(out_dram, t, j), x_flat(u, j * TPIX, TPIX)).then_inc(out_stored[j], 16)

            def store_chunk(t, u, k):
                act.wait_ge(out_ready[k], t + 1)
                act.dma_start(out_dram[t, :, k * CPIX:(k + 1) * CPIX],
                              x_flat(u, k * CPIX, CPIX)).then_inc(out_stored[k * THIRDS // CHUNKS], 16)

            def evacuate(t, u, k):
                last_image = isinstance(t, int) and t == IMAGES - 1
                if last_image:
                    store_chunk(t, u, k - 1)
                if on_act(t, k):
                    g = t * CHUNKS + k
                    act.wait_ge(chunk_mixed, g + 1)
                    act.wait_ge(bias_ready, t + 1)
                    if k < CHUNKS - 1:
                        act.wait_ge(s_summed, g + 2)
                    nc.scalar.activation(x_flat(u, k * CPIX, CPIX), ps_half(k), ACT.Identity,
                                         bias=bias[u % 2][:, :]).then_inc(out_ready[k], 1)
                if last_image:
                    store_chunk(t, u, k)
                else:
                    store(t, u, k * THIRDS // CHUNKS)

            take_moments(0, 0)
            for j in range(THIRDS):
                square_third(0, 0, j)
            guess_rstd(0)
            exp_gate(0)
            sum_third(1, 1, 2)
            take_moments(1, 1)
            for j in range(THIRDS):
                square_third(1, 1, j)

            def image(t, u, first, no_third, no_second, no_next):
                if not first:
                    evacuate(t - 1, u - 1, 5)
                if not no_second:
                    sum_third(t + 2, u + 2, 1)
                    sum_third(t + 2, u + 2, 2)
                evacuate(t, u, 1)
                if not no_next:
                    guess_rstd(t + 1)
                if not no_third:
                    sum_third(t + 3, u + 3, 0)
                if not no_second:
                    take_moments(t + 2, u + 2)
                    square_third(t + 2, u + 2, 0)
                evacuate(t, u, 3)
                if not no_next:
                    exp_gate(t + 1)
                if not no_second:
                    square_third(t + 2, u + 2, 1)
                    square_third(t + 2, u + 2, 2)

            for_images(act, image)
            evacuate(IMAGES - 1, SLOTS - 1, 5)
            for j in range(THIRDS):
                act.wait_ge(out_stored[j], 16 * (IMAGES + 1))

        @block.gpsimd
        def _(pool):
            EDGE_STEPS = 10

            def edges(t, u):
                e, r = edge[u % 2], top[u % 2]
                mean = column(moments, u, 2)
                pool.wait_ge(moments_ready, t * 2 + 2)
                for j in range(THIRDS):
                    pool.wait_ge(x_in[j], t * 16 + 16)
                col = x_rows(u, 0, H)[:, :, 0]
                row = x_rows(u, 0, 1)[:, 0, :]
                nc.gpsimd.tensor_tensor(corner[:, :], row[:, 0:1], mean, ALU.add).then_inc(edge_steps, 1)
                nc.gpsimd.tensor_scalar(half_col[:, :], col, 0.5, 0.0, ALU.mult, ALU.add).then_inc(edge_steps, 1)
                nc.gpsimd.tensor_scalar(e[:, 1:H, 1], col[:, 1:H], mean, K_EDGE, ALU.add, ALU.mult).then_inc(edge_steps, 1)
                nc.gpsimd.tensor_scalar(row_15[:, :], row, 1.5, 0.0, ALU.mult, ALU.add).then_inc(edge_steps, 1)
                nc.gpsimd.tensor_scalar(r[:, 0, 0:1], row[:, 0:1], 3.0, 0.0, ALU.mult, ALU.add).then_inc(edge_steps, 1)
                nc.gpsimd.tensor_scalar(r[:, 1, 1:W], row[:, 1:W], mean, K_EDGE, ALU.add, ALU.mult).then_inc(edge_steps, 1)
                pool.wait_ge(edge_steps, t * EDGE_STEPS + 6)
                nc.gpsimd.tensor_tensor(e[:, 1:H, 0], half_col[:, 1:H], half_col[:, 0:H - 1], ALU.add).then_inc(edge_steps, 1)
                nc.gpsimd.tensor_tensor(r[:, 0, 1:W], row_15[:, 1:W], row_15[:, 0:W - 1], ALU.add).then_inc(edge_steps, 1)
                nc.gpsimd.tensor_scalar(r[:, 1, 0:1], corner[:, :], K_CORNER, 0.0, ALU.mult, ALU.add).then_inc(edge_steps, 1)
                pool.wait_ge(edge_steps, t * EDGE_STEPS + 9)
                nc.gpsimd.tensor_tensor(r[:, 0, 1:2], r[:, 0, 1:2], r[:, 1, 0:1], ALU.add).then_inc(edge_steps, 1)

            def edges_up(t, u):
                pool.wait_ge(edge_steps, t * EDGE_STEPS + EDGE_STEPS)
                without_x = [k for k in range(CHUNKS) if on_act(t, k)]
                for k in without_x:
                    cells = edge[u % 2][:, k * ROWS:(k + 1) * ROWS, 0]
                    nc.gpsimd.tensor_tensor(cells, cells, x_rows(u, k * ROWS - 1, ROWS)[:, :, 0],
                                            ALU.add).then_inc(edges_done, 1)
                if without_x:
                    pool.wait_ge(edges_done, taken_out(t, CHUNKS - 1, True))

            def fix(t, u, k):
                g = t * CHUNKS + k
                s = s_rows(k)
                e = edge[u % 2][:, k * ROWS:(k + 1) * ROWS, :]
                pool.wait_ge(s_summed, g + 1)
                if k == 0:
                    nc.gpsimd.tensor_tensor(s[:, 1:ROWS, 0:2], s[:, 1:ROWS, 0:2], e[:, 1:ROWS, :], ALU.add).then_inc(top_fixed, 1)
                    nc.gpsimd.tensor_copy(s[:, 0, :], top[u % 2][:, 0, :]).then_inc(top_fixed, 1)
                    pool.wait_ge(top_fixed, t * 2 + 2)
                    nc.gpsimd.tensor_tensor(s[:, 1, :], s[:, 1, :], top[u % 2][:, 1, :], ALU.add).then_inc(s_ready, 1)
                elif on_act(t, k):
                    nc.gpsimd.tensor_tensor(s[:, :, 1], s[:, :, 1], e[:, :, 1], ALU.add).then_inc(s_ready, 1)
                    nc.gpsimd.tensor_copy(s[:, :, 0], e[:, :, 0]).then_inc(s_ready, 1)
                else:
                    nc.gpsimd.tensor_tensor(s[:, :, 0:2], s[:, :, 0:2], e, ALU.add).then_inc(s_ready, 1)

            edges(0, 0)
            edges_up(0, 0)
            for k in range(LEAD):
                fix(0, 0, k)

            def image(t, u, first, no_third, no_second, no_next):
                for k in range(CHUNKS):
                    if k == 0 and not no_next:
                        edges(t + 1, u + 1)
                    if k == 1 and not no_next:
                        edges_up(t + 1, u + 1)
                    if k + LEAD < CHUNKS:
                        fix(t, u, k + LEAD)
                    elif not no_next:
                        fix(t + 1, u + 1, k + LEAD - CHUNKS)

            for_images(pool, image)

        @block.vector
        def _(dve):
            def vertical(t, u, k):
                g = t * CHUNKS + k
                s = s_rows(k)
                dve.wait_ge(x_in[k * THIRDS // CHUNKS], t * 16 + 16)
                if not isinstance(t, int) or g >= SBUFS:
                    dve.wait_ge(chunk_mixed, g - SBUFS + 1)
                if on_act(t, k):
                    nc.vector.tensor_tensor(s[:, :, 1:W], x_rows(u, k * ROWS - 1, ROWS)[:, :, 1:W],
                                            x_rows(u, k * ROWS, ROWS)[:, :, 0:W - 1], ALU.add).then_inc(s_summed, 1)
                else:
                    skip = W if k == 0 else 0
                    nc.vector.tensor_tensor(s_buf[k % SBUFS][:, skip:CPIX], x_flat(u, k * CPIX + skip, CPIX - skip),
                                            x_flat(u, k * CPIX + skip - W, CPIX - skip), ALU.add).then_inc(vertical_done, 1)

            def horizontal(t, u, k):
                if on_act(t, k):
                    return
                s = s_rows(k)
                skip = 1 if k == 0 else 0
                dve.wait_ge(vertical_done, taken_out(t, k, False))
                cells = s[:, skip:ROWS, 1:W]
                nc.vector.tensor_tensor(cells, cells, x_rows(u, k * ROWS + skip, ROWS - skip)[:, :, 0:W - 1],
                                        ALU.add).then_inc(s_summed, 1)

            def evacuate(t, u, k):
                if on_act(t, k):
                    return
                dve.wait_ge(chunk_mixed, t * CHUNKS + k + 1)
                if k == 0:
                    dve.wait_ge(bias_ready, t + 1)
                if k < CHUNKS - 1:
                    dve.wait_ge(s_summed, t * CHUNKS + k + 2)
                cells = x_flat(u, k * CPIX, CPIX)
                nc.vector.scalar_tensor_tensor(out=cells, in0=ps_half(k), scalar=bias[u % 2][:, :], in1=cells,
                                               op0=ALU.add, op1=ALU.add).then_inc(out_ready[k], 1)

            def take_var(t):
                dve.wait_ge(var_mixed, t + 1)
                nc.vector.tensor_scalar(thirds_var[:, :], ps_gate[:, 4:4 + THIRDS], -1.0, EPS, ALU.mult, ALU.add,
                                        accum_out=var[:, :]).then_inc(var_ready, 1)

            def refine_rstd(t, u):
                dve.wait_ge(guess_ready, t + 1)
                nc.vector.scalar_tensor_tensor(out=vgg[:, :], in0=guess[:, :], scalar=guess[:, :], in1=var[:, :],
                                               op0=ALU.mult, op1=ALU.mult).then_inc(rstd_steps, 1)
                dve.wait_ge(rstd_steps, t * 3 + 1)
                nc.vector.tensor_scalar(newton[:, :], vgg[:, :], -0.5, 1.5, ALU.mult, ALU.add).then_inc(rstd_steps, 1)
                dve.wait_ge(rstd_steps, t * 3 + 2)
                nc.vector.tensor_tensor(rstd[:, :], guess[:, :], newton[:, :], ALU.mult).then_inc(rstd_steps, 1)
                dve.wait_ge(rstd_steps, t * 3 + 3)
                nc.vector.tensor_tensor(pooled[:, :], rstd[:, :], column(moments, u, 2, 1), ALU.mult).then_inc(pooled_ready, 1)

            def take_hidden(t):
                dve.wait_ge(hidden_mixed, t + 1)
                nc.vector.tensor_scalar(hidden[:, :], ps_gate[0:HID, 1:2], 0.0, None, ALU.max).then_inc(hidden_ready, 1)

            def scale_weights(t, u):
                dve.wait_ge(expz_ready, t + 1)
                nc.vector.tensor_scalar(expz1[:, :], expz[:, :], 1.0, None, ALU.add).then_inc(gate_steps, 1)
                dve.wait_ge(gate_steps, t * 3 + 1)
                nc.vector.reciprocal(gate[:, :], expz1[:, :]).then_inc(gate_steps, 1)
                dve.wait_ge(gate_steps, t * 3 + 2)
                nc.vector.tensor_scalar(scale[:, :], gate[:, :], rstd[:, :], 1.0 / 3.0, ALU.mult, ALU.mult).then_inc(gate_steps, 1)
                dve.wait_ge(gate_steps, t * 3 + 3)
                if not isinstance(t, int) or t >= 2:
                    dve.wait_ge(chunk_mixed, (t - 1) * CHUNKS)
                nc.vector.tensor_scalar(w_scaled[u % 2][:, :], gcn_w[:, :], scale[:, :], None, ALU.mult).then_inc(w_ready, 1)
                nc.vector.scalar_tensor_tensor(out=w_plus_eye[u % 2][:, :], in0=gcn_w[:, :], scalar=scale[:, :],
                                               in1=eye[:, :], op0=ALU.mult, op1=ALU.add).then_inc(w_ready, 1)

            def take_bias(t, u):
                dve.wait_ge(bias_mixed, t + 1)
                nc.vector.tensor_scalar(bias[u % 2][:, :], ps_gate[:, 3:4], 3.0, gcn_b[:, :], ALU.mult,
                                        ALU.add).then_inc(bias_ready, 1)

            def sum_third(t, u, j):
                dve.wait_ge(x_in[j], t * 16 + 16)
                if t:
                    dve.wait_ge(sums_done, t * THIRDS + j)
                nc.vector.reduce_sum(column(sums, u, THIRDS, j), x_flat(u, j * TPIX, TPIX),
                                     axis=mybir.AxisListType.X).then_inc(sums_done, 1)

            for j in range(THIRDS):
                sum_third(0, 0, j)
            for k in range(2):
                vertical(0, 0, k)
                horizontal(0, 0, k)
            sum_third(1, 1, 0)
            sum_third(1, 1, 1)
            dve.wait_ge(params_in, N_PARAMS)
            take_var(0)
            refine_rstd(0, 0)
            take_hidden(0)
            scale_weights(0, 0)
            for k in range(2, LEAD):
                vertical(0, 0, k)
                horizontal(0, 0, k)

            def image(t, u, first, no_third, no_second, no_next):
                for k in range(CHUNKS):
                    ahead = (t, u, k + LEAD) if k + LEAD < CHUNKS else (t + 1, u + 1, k + LEAD - CHUNKS)
                    adds = k + LEAD < CHUNKS or not no_next
                    if k == 0:
                        take_bias(t, u)
                    if adds:
                        vertical(*ahead)
                    if k == 0 and first:
                        sum_third(t + 2, u + 2, 0)
                    if k == 2 and not no_next:
                        refine_rstd(t + 1, u + 1)
                    if k == 4 and not no_next:
                        scale_weights(t + 1, u + 1)
                    evacuate(t, u, k)
                    if adds:
                        horizontal(*ahead)
                    if k == 1 and not no_next:
                        take_var(t + 1)
                    if k == 2 and not no_next:
                        take_hidden(t + 1)

            for_images(dve, image)

        @block.tensor
        def _(pe):
            def mix_mean(t, u):
                pe.wait_ge(sums_done, t * THIRDS + THIRDS)
                if not isinstance(t, int) or t:
                    pe.wait_ge(moments_ready, t * 2)
                for n, mix in enumerate((mean_mix, dev_mix)):
                    last = nc.tensor.matmul(ps_mean[:, n * THIRDS:(n + 1) * THIRDS], mix[:, :], columns(sums, u),
                                            start=True, stop=True)
                last.then_inc(mean_mixed, 1)

            def mix_var(t, u):
                pe.wait_ge(squares_done, t * THIRDS + THIRDS)
                if not isinstance(t, int) or t:
                    pe.wait_ge(bias_ready, t)
                nc.tensor.matmul(ps_gate[:, 4:4 + THIRDS], mean_mix[:, :], columns(squares, u), start=True,
                                 stop=True).then_inc(var_mixed, 1)

            def mix_hidden(t):
                pe.wait_ge(pooled_ready, t + 1)
                nc.tensor.matmul(ps_gate[0:HID, 1:2], fc1[:, :], pooled[:, :], start=True, stop=True).then_inc(hidden_mixed, 1)

            def mix_gate(t):
                pe.wait_ge(hidden_ready, t + 1)
                nc.tensor.matmul(ps_gate[:, 2:3], fc2[:, :], hidden[:, :], start=True, stop=True).then_inc(gate_mixed, 1)

            def mix_bias(t, u):
                pe.wait_ge(w_ready, t * 2 + 2)
                nc.tensor.matmul(ps_gate[:, 3:4], w_scaled[u % 2][:, :], column(moments, u, 2), start=True,
                                 stop=True).then_inc(bias_mixed, 1)

            def mix_chunk(t, u, k, first, after):
                g = t * CHUNKS + k
                pe.wait_ge(s_ready, t * CHUNKS + k + 1 + taken_out(t, k, True))
                if k >= 2:
                    before, image = k - 2, t
                else:
                    before, image = k + CHUNKS - 2, t - 1
                if k >= 2 or not first:
                    pe.wait_ge(out_ready[before], image + 1)
                half = ps_half(k)
                for b in range(BANKS):
                    bank = half[:, b * BANK:(b + 1) * BANK]
                    last = nc.tensor.matmul(bank, w_scaled[u % 2][:, :], s_buf[k % SBUFS][:, b * BANK:(b + 1) * BANK],
                                            start=True, stop=not on_act(t, k))
                    if on_act(t, k):
                        last = nc.tensor.matmul(bank, w_plus_eye[u % 2][:, :], x_flat(u, k * CPIX + b * BANK, BANK),
                                                start=False, stop=True)
                    if b == BANKS - 1:
                        last.then_inc(chunk_mixed, 1)
                    for f in after.get((k, b), ()):
                        f()

            pe.wait_ge(params_in, N_PARAMS)
            mix_mean(0, 0)
            mix_var(0, 0)
            mix_hidden(0)
            mix_gate(0)
            mix_bias(0, 0)
            mix_mean(1, 1)

            def image(t, u, first, no_third, no_second, no_next):
                after = {}
                if not no_next:
                    after[(1, 0)] = [lambda: mix_var(t + 1, u + 1)]
                    after[(3, 0)] = [lambda: mix_hidden(t + 1)]
                    after[(3, 2)] = [lambda: mix_gate(t + 1)]
                    after[(5, 1)] = [lambda: mix_bias(t + 1, u + 1)]
                if not no_second:
                    after[(2, 2)] = [lambda: mix_mean(t + 2, u + 2)]
                for k in range(CHUNKS):
                    mix_chunk(t, u, k, first, after)

            for_images(pe, image)


def kernel(x, L0_conv_w_fc1, L0_conv_w_fc2, L0_conv_gcn_w, L0_conv_gcn_b):
    import concourse.bacc as bacc
    from concourse.bass_utils import run_bass_kernel_spmd

    group = np.kron(np.eye(CH // GROUP), np.ones((GROUP, GROUP))) / GROUP
    arrays = {
        "x": np.ascontiguousarray(x).reshape(IMAGES, CH, PIX),
        "fc1": np.ascontiguousarray(np.asarray(L0_conv_w_fc1).T),
        "fc2": np.ascontiguousarray(np.asarray(L0_conv_w_fc2).T),
        "gcn_w": np.ascontiguousarray(L0_conv_gcn_w),
        "gcn_b": np.ascontiguousarray(L0_conv_gcn_b).reshape(CH, 1),
        "mean_mix": (-group / PIX).astype(np.float32),
        "dev_mix": ((np.eye(CH) - group) / PIX).astype(np.float32),
        "eye": np.eye(CH, dtype=np.float32),
    }
    nc = bacc.Bacc("TRN2", target_bir_lowering=False, num_devices=1)
    args = [nc.dram_tensor("in_" + n, a.shape, mybir.dt.from_np(a.dtype), kind="ExternalInput").ap() for n, a in arrays.items()]
    out = nc.dram_tensor("out", (IMAGES, CH, PIX), mybir.dt.float32, kind="ExternalOutput").ap()
    gated_grid_gcn(nc, *args, out)
    r = run_bass_kernel_spmd(nc, [{"in_" + n: a for n, a in arrays.items()}], core_ids=[0])
    return r.results[0]["out"].reshape(IMAGES, CH, H, W)
```
